# Optimizing a Trainium2 kernel written in Bass

```python
import numpy as np
import jax
import jax.numpy as jnp

def _softmax(x, axis=-1):
    return jax.nn.softmax(x, axis=axis)

def _gelu(x):
    return jax.nn.gelu(x, approximate=True)

def _silu(x):
    return jax.nn.silu(x)

def _sigmoid(x):
    return jax.nn.sigmoid(x)

def _layernorm(x, axis=-1, eps=1e-05):
    m = jnp.mean(x, axis=axis, keepdims=True)
    v = jnp.var(x, axis=axis, keepdims=True)
    return (x - m) / jnp.sqrt(v + eps)

def _scatter_add(tgt, idx, src, axis=0):
    return tgt.at[idx].add(src)

def _segment_sum(src, seg, n):
    return jax.ops.segment_sum(src, seg, n)
kernel_name = 'mk_gnn_resnorm_d1_gnn_r8_23a17b'

def setup_inputs(seed: int=0):
    np.random.seed(seed)
    _w = jnp.asarray

    def _rec_inputs():
        import jax
        import jax.numpy as jnp
        _gk = jax.random.key(seed)
        x = -0.000202 + 1 * jax.random.normal(jax.random.fold_in(_gk, 1), (12500, 160), jnp.float32)
        src = jax.random.randint(jax.random.fold_in(_gk, 2), (400000,), 0, 12500, jnp.int32)
        dst = jax.random.randint(jax.random.fold_in(_gk, 3), (400000,), 0, 12500, jnp.int32)
        _o = jnp.argsort(dst, stable=True)
        src = src[_o]
        dst = dst[_o]
        edge_attr_4 = 0.0012443 + 1.0001 * jax.random.normal(jax.random.fold_in(_gk, 12), (400000, 4), jnp.float32)
        edge_attr_64 = 0.000127647 + 1.00004 * jax.random.normal(jax.random.fold_in(_gk, 13), (400000, 64), jnp.float32)
        node_vec1 = jax.random.uniform(jax.random.fold_in(_gk, 14), (12500, 1), jnp.float32, 0.0, 1)
        return (x, src, dst, edge_attr_4, edge_attr_64, node_vec1)
    x, src, dst, edge_attr_4, edge_attr_64, node_vec1 = _rec_inputs()

    def _L0_gnn_setup():
        import jax, jax.numpy as jnp
        import numpy as np
        N, E = (5000, 80000)
        S_IN, V_IN = (64, 32)
        S_MID, V_MID = (96, 128)
        S_OUT, V_OUT = (96, 32)
        R = 64
        FC_HID = 64
        W_NUMEL = 64 + 64 + 32 + 32 + 32
        NUM_NEIGHBORS = 16.0

        def _inv(d):
            return 1.0 / jnp.sqrt(jnp.float32(d))

        def _forward(node_features, node_attr, edge_attr, edge_scalars, lin1_ws, lin1_wv, fc_w1, fc_w2, sc_ws, sc_wv, lin2_ws, lin2_wv, edge_src, edge_dst):
            n = node_features.shape[0]
            s = node_features[:, :S_IN]
            v = node_features[:, S_IN:].reshape(n, V_IN, 3)
            a = node_attr
            sc_s = s @ sc_ws * a * _inv(S_IN)
            sc_v = jnp.einsum('nci,cd->ndi', v, sc_wv) * a[:, :, None] * _inv(V_IN)
            h_s = s @ lin1_ws * a * _inv(S_IN)
            h_v = jnp.einsum('nci,cd->ndi', v, lin1_wv) * a[:, :, None] * _inv(V_IN)
            hid = jax.nn.silu(edge_scalars @ fc_w1 * _inv(R))
            w = hid @ fc_w2 * _inv(FC_HID)
            w1, w2, w3, w4, w5 = jnp.split(w, [64, 128, 160, 192], axis=-1)
            es = h_s[edge_src]
            ev = h_v[edge_src]
            e0 = edge_attr[:, :1]
            e1 = edge_attr[:, 1:4]
            m_s1 = w1 * es * e0
            m_s2 = w4 * jnp.einsum('eci,ei->ec', ev, e1) * _inv(3)
            m_v1 = (w2 * es)[:, :, None] * e1[:, None, :]
            m_v2 = w3[:, :, None] * ev * e0[:, :, None]
            m_v3 = w5[:, :, None] * jnp.cross(ev, e1[:, None, :]) * _inv(2)
            mid_s = jnp.concatenate([m_s1, m_s2], axis=-1)
            mid_v = jnp.concatenate([m_v1, m_v2, m_v3], axis=1)
            inv_nn = 1.0 / jnp.sqrt(jnp.float32(NUM_NEIGHBORS))
            agg_s = jax.ops.segment_sum(mid_s, edge_dst, num_segments=n) * inv_nn
            agg_v = jax.ops.segment_sum(mid_v, edge_dst, num_segments=n) * inv_nn
            o_s = agg_s @ lin2_ws * a * _inv(S_MID)
            o_v = jnp.einsum('nci,cd->ndi', agg_v, lin2_wv) * a[:, :, None] * _inv(V_MID)
            pre_s = sc_s + o_s
            pre_v = sc_v + o_v
            scalars = jax.nn.silu(pre_s[:, :64])
            gates = jax.nn.sigmoid(pre_s[:, 64:96])
            gated = gates[:, :, None] * pre_v
            return jnp.concatenate([scalars, gated.reshape(n, 3 * V_OUT)], axis=-1)
        key = jax.random.key(seed)
        ks = jax.random.split(key, 13)
        return {'node_features': jax.random.normal(ks[0], (N, S_IN + 3 * V_IN), jnp.float32), 'node_attr': jnp.ones((N, 1), jnp.float32), 'edge_src': jax.random.randint(ks[1], (E,), 0, N), 'edge_dst': jax.random.randint(ks[2], (E,), 0, N), 'edge_attr': jax.random.normal(ks[3], (E, 4), jnp.float32), 'edge_scalars': jax.random.normal(ks[4], (E, R), jnp.float32), 'lin1_ws': jax.random.normal(ks[5], (S_IN, S_IN), jnp.float32), 'lin1_wv': jax.random.normal(ks[6], (V_IN, V_IN), jnp.float32), 'fc_w1': jax.random.normal(ks[7], (R, FC_HID), jnp.float32), 'fc_w2': jax.random.normal(ks[8], (FC_HID, W_NUMEL), jnp.float32), 'sc_ws': jax.random.normal(ks[9], (S_IN, S_OUT), jnp.float32), 'sc_wv': jax.random.normal(ks[10], (V_IN, V_OUT), jnp.float32), 'lin2_ws': jax.random.normal(ks[11], (S_MID, S_OUT), jnp.float32), 'lin2_wv': jax.random.normal(ks[12], (V_MID, V_OUT), jnp.float32)}
    _L0_gnn_all = _L0_gnn_setup()
    _L0_gnn_in = {k: v for k, v in _L0_gnn_all.items() if k in ('lin1_ws', 'lin1_wv', 'fc_w1', 'fc_w2', 'sc_ws', 'sc_wv', 'lin2_ws', 'lin2_wv')}
    del _L0_gnn_all
    return {'x': x, 'src': src, 'dst': dst, 'edge_attr_4': edge_attr_4, 'edge_attr_64': edge_attr_64, 'node_vec1': node_vec1, 'L0_gnn_lin1_ws': _L0_gnn_in['lin1_ws'], 'L0_gnn_lin1_wv': _L0_gnn_in['lin1_wv'], 'L0_gnn_fc_w1': _L0_gnn_in['fc_w1'], 'L0_gnn_fc_w2': _L0_gnn_in['fc_w2'], 'L0_gnn_sc_ws': _L0_gnn_in['sc_ws'], 'L0_gnn_sc_wv': _L0_gnn_in['sc_wv'], 'L0_gnn_lin2_ws': _L0_gnn_in['lin2_ws'], 'L0_gnn_lin2_wv': _L0_gnn_in['lin2_wv']}

def reference(x, src, dst, edge_attr_4, edge_attr_64, node_vec1, L0_gnn_lin1_ws, L0_gnn_lin1_wv, L0_gnn_fc_w1, L0_gnn_fc_w2, L0_gnn_sc_ws, L0_gnn_sc_wv, L0_gnn_lin2_ws, L0_gnn_lin2_wv):
    import jax
    import jax.numpy as jnp

    def _L0_gnn_ref(node_features, node_attr, edge_src, edge_dst, edge_attr, edge_scalars, lin1_ws, lin1_wv, fc_w1, fc_w2, sc_ws, sc_wv, lin2_ws, lin2_wv):
        import jax, jax.numpy as jnp
        import numpy as np
        N, E = (5000, 80000)
        S_IN, V_IN = (64, 32)
        S_MID, V_MID = (96, 128)
        S_OUT, V_OUT = (96, 32)
        R = 64
        FC_HID = 64
        W_NUMEL = 64 + 64 + 32 + 32 + 32
        NUM_NEIGHBORS = 16.0

        def _inv(d):
            return 1.0 / jnp.sqrt(jnp.float32(d))

        def _forward(node_features, node_attr, edge_attr, edge_scalars, lin1_ws, lin1_wv, fc_w1, fc_w2, sc_ws, sc_wv, lin2_ws, lin2_wv, edge_src, edge_dst):
            n = node_features.shape[0]
            s = node_features[:, :S_IN]
            v = node_features[:, S_IN:].reshape(n, V_IN, 3)
            a = node_attr
            sc_s = s @ sc_ws * a * _inv(S_IN)
            sc_v = jnp.einsum('nci,cd->ndi', v, sc_wv) * a[:, :, None] * _inv(V_IN)
            h_s = s @ lin1_ws * a * _inv(S_IN)
            h_v = jnp.einsum('nci,cd->ndi', v, lin1_wv) * a[:, :, None] * _inv(V_IN)
            hid = jax.nn.silu(edge_scalars @ fc_w1 * _inv(R))
            w = hid @ fc_w2 * _inv(FC_HID)
            w1, w2, w3, w4, w5 = jnp.split(w, [64, 128, 160, 192], axis=-1)
            es = h_s[edge_src]
            ev = h_v[edge_src]
            e0 = edge_attr[:, :1]
            e1 = edge_attr[:, 1:4]
            m_s1 = w1 * es * e0
            m_s2 = w4 * jnp.einsum('eci,ei->ec', ev, e1) * _inv(3)
            m_v1 = (w2 * es)[:, :, None] * e1[:, None, :]
            m_v2 = w3[:, :, None] * ev * e0[:, :, None]
            m_v3 = w5[:, :, None] * jnp.cross(ev, e1[:, None, :]) * _inv(2)
            mid_s = jnp.concatenate([m_s1, m_s2], axis=-1)
            mid_v = jnp.concatenate([m_v1, m_v2, m_v3], axis=1)
            inv_nn = 1.0 / jnp.sqrt(jnp.float32(NUM_NEIGHBORS))
            agg_s = jax.ops.segment_sum(mid_s, edge_dst, num_segments=n) * inv_nn
            agg_v = jax.ops.segment_sum(mid_v, edge_dst, num_segments=n) * inv_nn
            o_s = agg_s @ lin2_ws * a * _inv(S_MID)
            o_v = jnp.einsum('nci,cd->ndi', agg_v, lin2_wv) * a[:, :, None] * _inv(V_MID)
            pre_s = sc_s + o_s
            pre_v = sc_v + o_v
            scalars = jax.nn.silu(pre_s[:, :64])
            gates = jax.nn.sigmoid(pre_s[:, 64:96])
            gated = gates[:, :, None] * pre_v
            return jnp.concatenate([scalars, gated.reshape(n, 3 * V_OUT)], axis=-1)
        return _forward(node_features, node_attr, edge_attr, edge_scalars, lin1_ws, lin1_wv, fc_w1, fc_w2, sc_ws, sc_wv, lin2_ws, lin2_wv, edge_src, edge_dst)
    x = _layernorm(x + _L0_gnn_ref(x, node_vec1, src, dst, edge_attr_4, edge_attr_64, L0_gnn_lin1_ws, L0_gnn_lin1_wv, L0_gnn_fc_w1, L0_gnn_fc_w2, L0_gnn_sc_ws, L0_gnn_sc_wv, L0_gnn_lin2_ws, L0_gnn_lin2_wv), axis=-1)
    return x

_drawn_inputs = setup_inputs


def setup_inputs(seed=0):
    import zlib

    import numpy as np

    out = dict(_drawn_inputs(seed))
    spreads = {}
    factors = {}
    for name, (base, spread) in spreads.items():
        noise = np.random.default_rng([zlib.crc32(name.encode()), seed]).standard_normal(out[name].shape)
        drawn = base * np.exp(spread * noise) if base else spread * noise
        out[name] = jnp.asarray(drawn.astype(out[name].dtype))
    for name, factor in factors.items():
        out[name] = (out[name] * factor).astype(out[name].dtype)
    return out
```

```python
from contextlib import ExitStack

import numpy as np

import concourse.bass as bass
from concourse import mybir

F32 = mybir.dt.float32
I32 = mybir.dt.int32
ALU = mybir.AluOpType
ACT = mybir.ActivationFunctionType
AX = mybir.AxisListType
ds = bass.ds

P = 128
N, E = 12500, 400000
S, V, HID = 64, 32, 64
F = S + 3 * V
SO = S + V
WN = 2 * S + 3 * V
PW = 2 * S + 9 * V
K4 = 4
AW = F
TW = AW - P
EPS = 1e-5

TILES = E // P
GT = 5
GROUPS = TILES // GT
PAIRS = GROUPS // 2
W = 32
GE = GT * P
CH = GE // 2
DUOS = 5
EARLY = 140
E4_FIRST = EARLY * 2 * GT
E4_PIECES = 115
E4_PIECE = (TILES - E4_FIRST) // E4_PIECES
assert E4_FIRST + E4_PIECES * E4_PIECE == TILES and 2 + E4_PIECES <= EARLY

NBLK = (N + P - 1) // P
LASTN = N - (NBLK - 1) * P
CB = 4
AGG_ROWS = 99 * P
SPARE = N + W

P_W2, P_W5, P_W4, P_W3, P_W1 = 0, 64, 160, 256, 352
W_ORDER = [(64, 64), (192, 32), (160, 32), (128, 32), (0, 64)]
PICK = [
    [(P_W3, 5, 1, 0)],
    [(P_W2, 2, 1, 0), (P_W5 + 32, 3, 1, 64)],
    [(P_W2, 2, 1, 0), (P_W5, 3, 2, 64)],
    [(P_W2, 4, 1, 0), (P_W4 + 64, 1, 1, 128)],
]

C_W = HID ** -0.5 * 16.0 ** -0.5
C_S = C_W * SO ** -0.5
C_V = C_W * P ** -0.5


class Shared:
    pass


def picked(prod, piece):
    start, blocks, step, _ = piece
    if step == 1:
        return prod[:, start:start + 32 * blocks]
    wide = prod[:, start:start + 32 * step * blocks].rearrange("p (b s c) -> p b s c", s=step, c=32)
    return wide[:, :, 0, :]


def setup_block(nc, io, m):
    with ExitStack() as ctx:
        def sb(name, shape, dt=F32):
            return ctx.enter_context(nc.sbuf_tensor(name, shape, dt))

        def sem(name):
            return ctx.enter_context(nc.semaphore(name))

        SLOTS = 4
        xs = sb("xs", [S, SLOTS, CB * P])
        xv = sb("xv", [3 * V, SLOTS, CB * P])
        hrow = sb("hrow", [P, SLOTS, CB, F])
        arow = sb("arow", [NBLK, P])
        iot = sb("iot", [P, P], I32)
        iotf = sb("iotf", [P, P])
        iot4 = sb("iot4", [P, K4, W], I32)
        iotw = sb("iotw", [P, W], I32)
        ones = sb("ones", [P, P])
        l1v = sb("l1v", [3 * V, V])
        l2v = sb("l2v", [P, V])
        l2g = sb("l2g", [3 * V, V])
        scv = sb("scv", [3 * V, V])
        lw1s = sb("lw1s", [S, S])
        lw1v = sb("lw1v", [3 * V, 3 * V])
        stage_s = sb("stage_s", [S, S])
        stage_sc = sb("stage_sc", [S, SO])
        stage_s1 = sb("stage_s1", [P, SO])
        stage_w4 = sb("stage_w4", [P, SO])
        basef = sb("basef", [1, GROUPS])
        baseb = sb("baseb", [P, GROUPS])
        delta = sb("delta", [P, GROUPS])
        ext = sb("ext", [P, 4])
        bad = sb("bad", [P, 6])
        badn = sb("badn", [1, 1])
        psh = [ctx.enter_context(nc.psum_tensor(f"psh{i}", [P, 2, 512], F32)) for i in range(2)]
        psb = ctx.enter_context(nc.psum_tensor("psb", [P, 2, 512], F32))
        psa = ctx.enter_context(nc.psum_tensor("psa", [P, 512], F32))
        psf = ctx.enter_context(nc.psum_tensor("psf", [P, 512], F32))

        s_lin1 = sem("lin1_loaded")
        s_w = sem("weights_loaded")
        s_node = sem("node_vec_loaded")
        s_dst = sem("dst_loaded")
        s_edge = sem("edge_columns_loaded")
        s_iota = sem("iotas_made")
        s_dve = sem("vector_steps")
        s_zero = sem("cleared")
        s_lw = sem("lin1_scaled")
        s_id = sem("identity_made")
        s_at = sem("node_vec_turned")
        s_a = sem("node_vec_ready")
        s_base = sem("base_row_ready")
        s_bb = sem("base_spread")
        s_bad = sem("misses_marked")
        s_badn = sem("misses_counted")
        s_xin = [sem(f"x_loaded{c}") for c in range(SLOTS)]
        s_hps = sem("h_in_psum")
        s_tick = sem("scalar_ticks")
        s_hcp = sem("h_copied")
        s_hout = [sem(f"h_stored{c}") for c in range(SLOTS)]

        chunks = NBLK // CB
        rounds = chunks // SLOTS
        rest = N - chunks * CB * P
        block = ctx.enter_context(nc.Block())

        loads = [
            (stage_sc[:], io["sc_ws"]),
            (stage_s1[P - V:P, :], io["lin2_ws"][0:V, :]), (stage_w4[0:V, :], io["lin2_ws"][V:S, :]),
            (l2v[0:S, :], io["lin2_wv"][0:S, :]),
            (l2v[S:S + V, :], io["lin2_wv"][S + V:S + 2 * V, :]),
            (l2v[S + V:P, :], io["lin2_wv"][S + V:S + 2 * V, :]),
        ]
        for i in range(3):
            r = slice(V * i, V * i + V)
            loads += [(scv[r, :], io["sc_wv"]), (l2g[r, :], io["lin2_wv"][S:S + V, :]),
                      (stage_w4[V * i + V:V * i + 2 * V, :], io["lin2_ws"][S:SO, :])]
        for half in range(2):
            r = slice(S * half, S * half + S)
            at = 0
            for src, width in W_ORDER:
                loads.append((m.fc2[r, at:at + width], io["fc_w2"][:, src:src + width]))
                at += width
        n_w = 16 * (len(loads) + 2)

        @block.sync
        def _(sp):
            sp.dma_start(stage_s[:], io["lin1_ws"]).then_inc(s_lin1, 16)
            for i in range(3):
                sp.dma_start(l1v[V * i:V * i + V, :], io["lin1_wv"]).then_inc(s_lin1, 16)
            sp.wait_ge(s_zero, 1)
            sp.dma_start(arow[0:NBLK - 1, :], io["node_vec"][0:(NBLK - 1) * P, :].rearrange("(b p) o -> b (p o)", p=P)).then_inc(s_node, 16)
            sp.dma_start(arow[NBLK - 1:NBLK, 0:LASTN], io["node_vec"][(NBLK - 1) * P:N, :].rearrange("p o -> o p")).then_inc(s_node, 16)

            def load_x(c, start, width):
                sp.dma_start(xs[:, c, 0:width], io["xT"][0:S, ds(start, width)]).then_inc(s_xin[c], 16)
                sp.dma_start(xv[:, c, 0:width], io["xT"][S:F, ds(start, width)]).then_inc(s_xin[c], 16)

            for c in range(SLOTS):
                load_x(c, c * CB * P, CB * P)
            sp.dma_start(m.dst[:], io["dstT"]).then_inc(s_dst, 16)
            with sp.Fori(1, rounds) as i:
                for c in range(SLOTS):
                    sp.wait_ge(s_hps, CB * (SLOTS * (i - 1) + c + 1))
                    sp.sem_inc(s_tick, 1)
                    load_x(c, (SLOTS * i + c) * (CB * P), CB * P)
            sp.wait_ge(s_hps, CB * (chunks - SLOTS + 1))
            load_x(0, chunks * CB * P, rest)
            sp.dma_start(m.e4[:, 0:E4_FIRST, :], io["e4T"][:, 0:E4_FIRST, :]).then_inc(s_edge, 16)
            sp.dma_start(m.src[:], io["srcT"]).then_inc(s_edge, 16)
            for c in range(SLOTS):
                sp.wait_ge(s_hout[c], 16 * (rounds + (2 if c == 0 else 0)))
            sp.wait_ge(s_edge, 32)

        @block.gpsimd
        def _(pool):
            nc.gpsimd.iota(iot[:], pattern=[[1, P]], base=0, channel_multiplier=-1).then_inc(s_iota, 1)
            nc.gpsimd.iota(iot4[:], pattern=[[-W, K4], [-1, W]], base=0, channel_multiplier=1).then_inc(s_iota, 1)
            nc.gpsimd.iota(iotw[:], pattern=[[1, W]], base=0, channel_multiplier=0).then_inc(s_iota, 1)
            nc.gpsimd.iota(m.spare[:], pattern=[[1, 1]], base=SPARE, channel_multiplier=1).then_inc(s_iota, 1)

        @block.vector
        def _(dve):
            step = [0]

            def then(ins):
                ins.then_inc(s_dve, 1)
                step[0] += 1
                dve.wait_ge(s_dve, step[0])

            then(nc.vector.memset(m.fc1[:], 0.0))
            nc.vector.memset(arow[:], 0.0).then_inc(s_zero, 1)
            dve.wait_ge(s_iota, 4)
            then(nc.vector.tensor_copy(iotf[:], iot[:]))
            then(nc.vector.tensor_scalar(m.ident[:], iotf[:], 0.0, None, ALU.is_equal))
            nc.vector.tensor_scalar(m.earlier[:], iotf[:], 0.0, None, ALU.is_lt).then_inc(s_id, 1)
            nc.vector.tensor_copy(m.win[:], iotw[:])
            nc.vector.memset(m.mv[:], 0.0)
            nc.vector.memset(m.m0[:], 0.0)
            nc.vector.memset(m.mscv[:], 0.0)
            nc.vector.memset(lw1v[:], 0.0)
            then(nc.vector.memset(ones[:], 1.0))
            for k in range(K4):
                for b in range(K4):
                    r = slice(W * b, W * b + W)
                    if b == k:
                        last = nc.vector.tensor_copy(m.shift[r, k, :], iot4[r, k, :])
                    else:
                        last = nc.vector.memset(m.shift[r, k, :], 1e6)
            then(last)
            dve.wait_ge(s_lin1, 64)
            nc.vector.tensor_scalar(lw1s[:], stage_s[:], S ** -0.5, None, ALU.mult)
            for i in range(3):
                r = slice(V * i, V * i + V)
                last = nc.vector.tensor_scalar(lw1v[r, r], l1v[r, :], V ** -0.5, None, ALU.mult)
            last.then_inc(s_lw, 1)
            dve.wait_ge(s_at, 1)
            nc.vector.tensor_copy(m.a[:], psa[:, 0:NBLK]).then_inc(s_a, 1)
            nc.vector.tensor_scalar(m.ahalf[:], psa[:, 0:NBLK], 0.5, None, ALU.mult)
            dve.wait_ge(s_w, n_w)
            nc.vector.tensor_scalar(m.mscs[:], stage_sc[:], S ** -0.5, None, ALU.mult)
            nc.vector.tensor_scalar(m.m0[P - V:P, 0:SO], stage_s1[P - V:P, :], C_S, None, ALU.mult)
            nc.vector.tensor_scalar(m.m4[0:V, :], stage_w4[0:V, :], C_S, None, ALU.mult)
            for i in range(1, 4):
                r = slice(V * i, V * i + V)
                nc.vector.tensor_scalar(m.m4[r, :], stage_w4[r, :], C_S * 3 ** -0.5, None, ALU.mult)

            def axis(t, r, i):
                return t[r, :].rearrange("p (d i) -> p d i", i=3)[:, :, i]

            for i in range(3):
                r = slice(V * i, V * i + V)
                nc.vector.tensor_scalar(axis(m.m0[:, SO:2 * SO], r, i), l2g[r, :], C_V, None, ALU.mult)
                nc.vector.tensor_scalar(axis(m.mscv, r, i), scv[r, :], V ** -0.5, None, ALU.mult)
                nc.vector.tensor_scalar(axis(m.mv[:, i, :], slice(0, S), i), l2v[0:S, :], C_V, None, ALU.mult)
                for j, a in enumerate(x for x in range(3) if x != i):
                    r = slice(S + V * j, S + V * j + V)
                    sign, to = (1, (i + 1) % 3) if a == (i + 2) % 3 else (-1, (i + 2) % 3)
                    last = nc.vector.tensor_scalar(axis(m.mv[:, i, :], r, to), l2v[r, :],
                                                   sign * C_V * 2 ** -0.5, None, ALU.mult)
            then(last)
            dve.wait_ge(s_dst, 16)
            then(nc.vector.tensor_copy(m.base[:], m.dst[0:1, 0:TILES:GT]))
            nc.vector.tensor_copy(basef[:], m.dst[0:1, 0:TILES:GT]).then_inc(s_base, 1)
            dve.wait_ge(s_bb, 1)
            half = GROUPS // 2 + 1
            nc.vector.tensor_copy(baseb[:, 0:half], psb[:, 0, 0:half])
            then(nc.vector.tensor_copy(baseb[:, half:GROUPS], psb[:, 1, 0:GROUPS - half]))
            nc.vector.memset(m.delta[:, 0:1], 0.0)
            then(nc.vector.tensor_tensor(m.delta[:, 1:GROUPS], baseb[:, 1:GROUPS], baseb[:, 0:GROUPS - 1], ALU.subtract))
            local = m.local[:].rearrange("p (g t) -> p g t", t=GT)
            then(nc.vector.tensor_tensor(local, m.dst[:].rearrange("p (g t) -> p g t", t=GT),
                                         baseb[:].unsqueeze(2).to_broadcast([P, GROUPS, GT]), ALU.subtract))
            nc.vector.tensor_reduce(ext[:, 0:1], m.local[:], AX.X, ALU.max)
            nc.vector.tensor_reduce(ext[:, 1:2], m.local[:], AX.X, ALU.min)
            nc.vector.tensor_reduce(ext[:, 2:3], m.delta[:], AX.X, ALU.max)
            then(nc.vector.tensor_reduce(ext[:, 3:4], m.delta[:], AX.X, ALU.min))
            nc.vector.tensor_scalar(bad[:, 0:1], ext[:, 0:1], float(W - 1), None, ALU.is_gt)
            nc.vector.tensor_scalar(bad[:, 1:2], ext[:, 1:2], 0.0, None, ALU.is_lt)
            nc.vector.tensor_scalar(bad[:, 2:3], ext[:, 2:3], float(W), None, ALU.is_gt)
            nc.vector.tensor_scalar(bad[:, 3:4], ext[:, 3:4], 0.0, None, ALU.is_lt)
            nc.vector.tensor_scalar(bad[:, 4:5], baseb[:, 0:1], 0.0, None, ALU.is_gt)
            nc.vector.tensor_scalar(bad[:, 5:6], baseb[:, GROUPS - 1:GROUPS], float(N - W), None, ALU.is_lt).then_inc(s_bad, 1)
            dve.wait_ge(s_badn, 1)
            then(nc.vector.tensor_reduce(badn[:], psf[0:1, 0:6], AX.X, ALU.add))
            then(nc.vector.tensor_copy(m.misses[:], badn[:]))
            nc.vector.memset(m.aggsb[:], 0.0)

        @block.tensor
        def _(pe):
            pe.wait_ge(s_id, 1)
            pe.wait_ge(s_node, 32)
            nc.tensor.transpose(psa[:, 0:NBLK], arow[:], m.ident[0:NBLK, 0:NBLK]).then_inc(s_at, 1)
            pe.wait_ge(s_lw, 1)

            def project(c, b, width):
                n = slice(b * P, b * P + width)
                out = psh[c % 2][0:width, b // 2, F * (b % 2):F * (b % 2) + F]
                nc.tensor.matmul(out[:, 0:S], xs[:, c, n], lw1s[:], start=True, stop=True)
                return nc.tensor.matmul(out[:, S:F], xv[:, c, n], lw1v[:], start=True, stop=True)

            def chunk(c, i, widths, free):
                pe.wait_ge(s_xin[c], 32 * (i + 1))
                if free:
                    pe.wait_ge(s_hcp, CB * (SLOTS * i + c - 1))
                for b, width in enumerate(widths):
                    project(c, b, width).then_inc(s_hps, 1)

            for c in range(SLOTS):
                chunk(c, 0, [P] * CB, c >= 2)
            pe.wait_ge(s_base, 1)
            half = GROUPS // 2 + 1
            nc.tensor.matmul(psb[:, 0, 0:half], ones[0:1, :], basef[:, 0:half], start=True, stop=True)
            nc.tensor.matmul(psb[:, 1, 0:GROUPS - half], ones[0:1, :], basef[:, half:GROUPS],
                             start=True, stop=True).then_inc(s_bb, 1)
            with pe.Fori(1, rounds) as i:
                for c in range(SLOTS):
                    chunk(c, i, [P] * CB, True)
            chunk(0, rounds, [P, LASTN], True)
            pe.wait_ge(s_bad, 1)
            nc.tensor.matmul(psf[0:1, 0:6], ones[:, 0:1], bad[:], start=True, stop=True).then_inc(s_badn, 1)

        @block.scalar
        def _(act):
            for dst, src in loads:
                act.dma_start(dst, src).then_inc(s_w, 16)
            act.wait_ge(s_zero, 1)
            for half in range(2):
                r = slice(S * half, S * half + S)
                act.dma_start(m.fc1[r, r], io["fc_w1"]).then_inc(s_w, 16)
            act.wait_ge(s_a, 1)

            def chunk(c, i, first):
                if not first:
                    act.wait_ge(s_hout[c], 16 * i)
                at = SLOTS * i + c
                for b in range(CB):
                    if b % 2 == 0:
                        act.wait_ge(s_hps, CB * at + b + 2)
                        act.sem_inc(s_tick, 1)
                    nc.scalar.activation(hrow[:, c, b, :], psh[c % 2][:, b // 2, F * (b % 2):F * (b % 2) + F], ACT.Copy,
                                         scale=m.a[:, ds(at * CB + b, 1)]).then_inc(s_hcp, 1)
                act.wait_ge(s_hcp, CB * (at + 1))
                act.dma_start(m.h[ds(at * (CB * P), CB * P), :].rearrange("(b p) f -> p b f", p=P),
                              hrow[:, c, :, :]).then_inc(s_hout[c], 16)

            for c in range(SLOTS):
                chunk(c, 0, True)
            with act.Fori(1, rounds) as i:
                for c in range(SLOTS):
                    chunk(c, i, False)
            act.wait_ge(s_hout[0], 16 * rounds)
            done = CB * chunks
            for b, width in enumerate([P, LASTN]):
                act.wait_ge(s_hps, done + 2)
                nc.scalar.activation(hrow[0:width, 0, b, :], psh[0][0:width, 0, F * b:F * b + F], ACT.Copy,
                                     scale=m.a[0:width, done + b:done + b + 1]).then_inc(s_hcp, 1)
            act.wait_ge(s_hcp, done + 2)
            act.dma_start(m.h[done * P:done * P + P, :], hrow[:, 0, 0, :]).then_inc(s_hout[0], 16)
            act.dma_start(m.h[done * P + P:N, :], hrow[0:LASTN, 0, 1, :]).then_inc(s_hout[0], 16)


def edge_block(nc, io, m):
    with ExitStack() as ctx:
        def sb(name, shape, dt=F32):
            return ctx.enter_context(nc.sbuf_tensor(name, shape, dt))

        def sem(name):
            return ctx.enter_context(nc.semaphore(name))

        es = sb("es", [P, 2, CH])
        hid = sb("hid", [P, 2 * CH])
        idx = sb("idx", [P, 2 * GT], I32)
        rows = sb("rows", [P, 2 * GT, F])
        prod = sb("prod", [P, 2 * GT, PW])
        hot = sb("hot", [P, 2 * GT, W])
        sel = sb("sel", [P, 2 * GT, K4, W])
        carry = sb("carry", [P, 2, K4, W])
        dstrow = sb("dstrow", [P, P], I32)
        same = sb("same", [P, P])
        before = sb("before", [P, P])
        nbefore = sb("nbefore", [P, 2])
        rowf = sb("rowf", [P, 2])
        row = sb("row", [P, 1], I32)
        gsel = sb("gsel", [P, K4, P])
        gsum = sb("gsum", [P, K4 * AW])

        psw = [ctx.enter_context(nc.psum_tensor(f"psw{d}", [P, 2, WN], F32)) for d in range(DUOS)]
        psh = ctx.enter_context(nc.psum_tensor("psx", [P, 512], F32))
        psg = [ctx.enter_context(nc.psum_tensor(f"psg{g}", [P, 512], F32)) for g in range(2)]

        e4_loaded = sem("e4_loaded")
        es_loaded = [sem(f"es_loaded{c}") for c in range(2)]
        hid_summed = sem("hid_summed")
        hid_ready = sem("hid_ready")
        w_ready = sem("w_ready")
        half_done = sem("half_done")
        idx_ready = sem("idx_ready")
        idx_seen = sem("idx_seen")
        loads_seen = sem("loads_seen")
        row_loaded = [sem(f"row_loaded{j}") for j in range(2 * GT)]
        hot_ready = sem("hot_ready")
        prod_ready = sem("prod_ready")
        carry_ready = [sem(f"carry_ready{g}") for g in range(2)]
        duo_summed = sem("duo_summed")
        group_summed = sem("group_summed")
        agg_copied = sem("agg_copied")
        agg_stored = [sem(f"agg_stored{g}") for g in range(2)]
        g_zero = sem("g_zero")
        g_cleared = sem("g_cleared")
        g_es = sem("g_es")
        g_dst = sem("g_dst")
        g_hid = sem("g_hid")
        g_act = sem("g_act")
        g_w = sem("g_w")
        g_idx = sem("g_idx")
        g_seen = sem("g_seen")
        g_rows = sem("g_rows")
        g_prod = sem("g_prod")
        g_step = sem("g_step")
        g_row = sem("g_row")
        g_sum = sem("g_sum")
        g_copy = sem("g_copy")
        g_added = sem("g_added")

        block = ctx.enter_context(nc.Block())

        def weigh(out, w, row):
            w543 = w[:, S:S + 3 * V].rearrange("p (w c) -> p w c", w=3)
            nc_out = out[:, P_W5:P_W1].rearrange("p (w i c) -> p w i c", w=3, i=3)
            ev = row[:, S:F].rearrange("p (i c) -> p i c", i=3)
            return nc.vector.tensor_tensor(nc_out, w543.unsqueeze(2).to_broadcast([P, 3, 3, V]),
                                           ev.unsqueeze(1).to_broadcast([P, 3, 3, V]), ALU.mult)

        def two_runs(t, first, second, n):
            ap = t[:, :, first:first + S].unsqueeze(2).to_broadcast([P, n, 2, S])
            steps = [list(x) for x in ap.ap]
            steps[2][0] = second - first
            return bass.AP(tensor=ap.tensor, offset=ap.offset, ap=steps)

        def weigh_scalars(out, w, row, n):
            return nc.vector.tensor_tensor(two_runs(out, P_W2, P_W1, n), two_runs(w, 0, S + 3 * V, n),
                                           row[:, :, 0:S].unsqueeze(2).to_broadcast([P, n, 2, S]), ALU.mult)

        @block.sync
        def _(sp):
            miss = sp.value_load(m.misses[0:1, 0:1], min_val=0, max_val=6 * P)

            def load(c, i, halves, free):
                if free:
                    sp.wait_ge(hid_summed, 2 * (i - 1) + c + 1)
                    sp.sem_inc(loads_seen, 1)
                for g in range(halves):
                    sp.dma_start(es[S * g:S * g + S, c, :],
                                 io["esT"][:, ds(i * (2 * GE) + g * GE + c * CH, CH)]).then_inc(es_loaded[c], 16)

            def store(g, i, first=False):
                at = sp.value_load(m.base[0:1, ds(2 * i + g, 1)], min_val=0, max_val=N - 1)
                sp.wait_ge(agg_copied, 2 * i + g + 1)
                sp.sem_inc(loads_seen, 1)
                if g:
                    sp.wait_ge(agg_stored[0], 32 * (i + 1))
                elif not first:
                    sp.wait_ge(agg_stored[1], 32 * i)
                sp.sem_inc(loads_seen, 1)
                window = m.agg[ds(at, W), :]
                sp.dma_start(window[:, 0:K4 * P].rearrange("n (k c) -> k n c", k=K4),
                             m.aggsb[:, g, 0:P]).then_inc(agg_stored[g], 16)
                sp.dma_start(window[:, K4 * P:K4 * AW].rearrange("n (k c) -> k n c", k=K4),
                             m.aggsb[:, g, P:AW]).then_inc(agg_stored[g], 16)

            def load_e4(q):
                tiles = ds(E4_FIRST + q * E4_PIECE, E4_PIECE)
                sp.dma_start(m.e4[:, tiles, :], io["e4T"][:, tiles, :]).then_inc(e4_loaded, 16)

            with sp.If(miss == 0):
                for c in range(2):
                    load(c, 0, 2, False)
                for c in range(2):
                    load(c, 1, 2, True)
                for c in range(2):
                    load(c, 2, 2, True)
                store(0, 0, True)
                store(1, 0)
                for start, end in ((2, 2 + E4_PIECES), (2 + E4_PIECES, PAIRS - 1)):
                    with sp.Fori(start, end) as i:
                        for c in range(2):
                            load(c, i + 1, 2, True)
                        if start == 2:
                            load_e4(i - 2)
                        store(0, i - 1)
                        store(1, i - 1)
                for c in range(2):
                    load(c, PAIRS, 1, True)
                for i in range(PAIRS - 2, PAIRS):
                    store(0, i)
                    store(1, i)
                store(0, PAIRS)
                sp.wait_ge(agg_stored[0], 32 * (PAIRS + 1))
                sp.wait_ge(agg_stored[1], 32 * PAIRS)
            with sp.Else():
                with sp.Fori(0, E4_PIECES) as q:
                    load_e4(q)
                sp.wait_ge(g_zero, 1)
                with sp.Fori(0, AGG_ROWS // P) as b:
                    sp.dma_start(m.agg[ds(b * P, P), :], gsum[:]).then_inc(g_cleared, 16)
                sp.wait_ge(g_cleared, 16 * (AGG_ROWS // P))

                def tile(t, first):
                    if not first:
                        sp.wait_ge(g_added, 16 * t)
                        sp.sem_inc(loads_seen, 1)
                    sp.dma_start(es[0:S, 0, 0:P], io["esT"][:, ds(t * P, P)]).then_inc(g_es, 16)
                    sp.dma_start(dstrow[:], io["dst"][ds(t, 1), :].to_broadcast([P, P])).then_inc(g_dst, 16)

                tile(0, True)
                with sp.Fori(1, TILES) as t:
                    tile(t, False)

        @block.gpsimd
        def _(pool):
            miss = pool.value_load(m.misses[0:1, 0:1], min_val=0, max_val=6 * P)

            def gather(i, tiles):
                for j in range(tiles):
                    if j % GT == 0:
                        pool.wait_ge(idx_ready, 2 * i + j // GT + 1)
                        pool.sem_inc(idx_seen, 1)
                    nc.gpsimd.indirect_dma_start(
                        out=rows[:, j, :], out_offset=None, in_=m.h,
                        in_offset=bass.IndirectOffsetOnAxis(ap=idx[:, j:j + 1], axis=0)).then_inc(row_loaded[j], 16)

            with pool.If(miss == 0):
                with pool.Fori(0, PAIRS) as i:
                    gather(i, 2 * GT)
                gather(PAIRS, GT)
            with pool.Else():
                with pool.Fori(0, TILES) as t:
                    pool.wait_ge(g_idx, t + 1)
                    pool.sem_inc(g_seen, 1)
                    nc.gpsimd.indirect_dma_start(
                        out=rows[:, 0, :], out_offset=None, in_=m.h,
                        in_offset=bass.IndirectOffsetOnAxis(ap=idx[:, 0:1], axis=0)).then_inc(g_rows, 16)
                    pool.wait_ge(g_copy, t + 1)
                    pool.sem_inc(g_seen, 1)
                    nc.gpsimd.indirect_dma_start(
                        out=m.agg, out_offset=bass.IndirectOffsetOnAxis(ap=row[:, 0:1], axis=0),
                        in_=gsum[:], in_offset=None, compute_op=ALU.add).then_inc(g_added, 16)

        @block.scalar
        def _(act):
            miss = act.value_load(m.misses[0:1, 0:1], min_val=0, max_val=6 * P)

            def activate(c, i, halves, free):
                act.wait_ge(hid_summed, 2 * i + c + 1)
                if free is not None:
                    act.wait_ge(w_ready, free)
                r = slice(0, S * halves)
                nc.scalar.activation(hid[r, CH * c:CH * c + CH], psh[r, 0:CH], ACT.Silu,
                                     scale=HID ** -0.5).then_inc(hid_ready, 1)

            def copy_out(g, i, free):
                act.wait_ge(group_summed, 2 * i + g + 1)
                if free:
                    act.wait_ge(agg_stored[g], 32 * i)
                nc.scalar.activation(m.aggsb[:, g, :], psg[g][:, 0:AW], ACT.Copy).then_inc(agg_copied, 1)

            with act.If(miss == 0):
                for c in range(2):
                    activate(c, 0, 2, None)
                for c in range(2):
                    activate(c, 1, 2, DUOS - 1 + c)
                copy_out(0, 0, False)
                copy_out(1, 0, False)
                with act.Fori(1, PAIRS - 1) as i:
                    for c in range(2):
                        activate(c, i + 1, 2, DUOS * i + DUOS - 1 + c)
                    copy_out(0, i, True)
                    copy_out(1, i, True)
                last = PAIRS - 1
                for c in range(2):
                    activate(c, PAIRS, 1, DUOS * last + DUOS - 1 + c)
                copy_out(0, last, True)
                copy_out(1, last, True)
                copy_out(0, PAIRS, True)
            with act.Else():
                with act.Fori(0, TILES) as t:
                    act.wait_ge(g_hid, t + 1)
                    nc.scalar.activation(hid[0:S, 0:P], psh[0:S, 0:P], ACT.Silu,
                                         scale=HID ** -0.5).then_inc(g_act, 1)
                    act.wait_ge(g_sum, t + 1)
                    for h, bank in enumerate(psg):
                        sums = bank[:, 0:2 * AW].rearrange("p (k c) -> p k c", k=2)
                        whole = gsum[:, 2 * P * h:2 * P * h + 2 * P].rearrange("p (k c) -> p k c", k=2)
                        apart = gsum[:, K4 * P + 2 * TW * h:K4 * P + 2 * TW * h + 2 * TW].rearrange("p (k c) -> p k c", k=2)
                        nc.scalar.activation(whole, sums[:, :, 0:P], ACT.Copy)
                        ins = nc.scalar.activation(apart, sums[:, :, P:AW], ACT.Copy)
                    ins.then_inc(g_copy, 1)

        @block.vector
        def _(dve):
            miss = dve.value_load(m.misses[0:1, 0:1], min_val=0, max_val=6 * P)

            def indices(half, i):
                return nc.vector.tensor_copy(idx[:, GT * half:GT * half + GT],
                                             m.src[:, ds(i * (2 * GT) + GT * half, GT)])

            def shift_matrix(g, i):
                return nc.vector.tensor_tensor(
                    carry[:, g, :, :], m.shift[:],
                    m.delta[:, ds(2 * i + g, 1)].unsqueeze(2).to_broadcast([P, K4, W]), ALU.is_equal
                ).then_inc(carry_ready[g], 1)

            def products(i, first, tiles, following):
                if not first:
                    dve.wait_ge(prod_ready, DUOS * i)
                nc.vector.tensor_tensor(
                    hot[:, 0:tiles, :], m.win[:].unsqueeze(1).to_broadcast([P, tiles, W]),
                    m.local[:, ds(i * (2 * GT), tiles)].unsqueeze(2).to_broadcast([P, tiles, W]),
                    ALU.is_equal).then_inc(hot_ready, 1)
                for d in range((tiles + 1) // 2):
                    n = min(2, tiles - 2 * d)
                    t = slice(2 * d, 2 * d + n)
                    if d == 0:
                        if not first:
                            dve.wait_ge(group_summed, 2 * i - 1)
                        shift_matrix(0, i)
                        dve.wait_ge(hot_ready, i + 1)
                    if not first:
                        dve.wait_ge(duo_summed, DUOS * (i - 1) + d + 1)
                    if d == DUOS - 1:
                        if not first:
                            dve.wait_ge(group_summed, 2 * i)
                        shift_matrix(1, i)
                    nc.vector.tensor_tensor(
                        sel[:, t, :, :], hot[:, t, :].unsqueeze(2).to_broadcast([P, n, K4, W]),
                        m.e4[:, ds(i * (2 * GT) + 2 * d, n), :].unsqueeze(3).to_broadcast([P, n, K4, W]), ALU.mult)
                    dve.wait_ge(w_ready, DUOS * i + d + 1)
                    for j in range(2 * d, 2 * d + n):
                        dve.wait_ge(row_loaded[j], 16 * (i + 1))
                    for j in range(2 * d, 2 * d + n):
                        weigh(prod[:, j, :], psw[d][:, j % 2, :], rows[:, j, :])
                    weigh_scalars(prod[:, t, :], psw[d][:, 0:n, :], rows[:, t, :], n).then_inc(prod_ready, 1)
                    if d == 2 and following:
                        indices(0, i + 1).then_inc(idx_ready, 1)
                    if d == 4 and following > GT:
                        indices(1, i + 1).then_inc(idx_ready, 1)

            with dve.If(miss == 0):
                indices(0, 0).then_inc(idx_ready, 1)
                indices(1, 0).then_inc(idx_ready, 1)
                products(0, True, 2 * GT, 2 * GT)
                with dve.Fori(1, EARLY) as i:
                    products(i, False, 2 * GT, 2 * GT)
                dve.wait_ge(e4_loaded, 16 * E4_PIECES)
                with dve.Fori(EARLY, PAIRS - 1) as i:
                    products(i, False, 2 * GT, 2 * GT)
                products(PAIRS - 1, False, 2 * GT, GT)
                products(PAIRS, False, GT, 0)
            with dve.Else():
                nc.vector.memset(gsum[:], 0.0).then_inc(g_zero, 1)
                dve.wait_ge(e4_loaded, 16 * E4_PIECES)
                STEPS = 6
                with dve.Fori(0, TILES) as t:
                    step = [0]

                    def then(ins):
                        ins.then_inc(g_step, 1)
                        step[0] += 1
                        dve.wait_ge(g_step, t * STEPS + step[0])

                    dve.wait_ge(g_es, 16 * (t + 1))
                    dve.wait_ge(g_dst, 16 * (t + 1))
                    nc.vector.tensor_tensor(same[:], dstrow[:], m.dst[:, ds(t, 1)].to_broadcast([P, P]), ALU.is_equal).then_inc(g_step, 1)
                    step[0] += 1
                    nc.vector.tensor_copy(idx[:, 0:1], m.src[:, ds(t, 1)]).then_inc(g_idx, 1)
                    dve.wait_ge(g_step, t * STEPS + step[0])
                    then(nc.vector.tensor_tensor(before[:], same[:], m.earlier[:], ALU.mult))
                    then(nc.vector.tensor_reduce(nbefore[:, 0:1], before[:], AX.X, ALU.max))
                    then(nc.vector.tensor_tensor(rowf[:, 0:1], m.spare[:], m.dst[:, ds(t, 1)], ALU.subtract))
                    then(nc.vector.tensor_tensor(rowf[:, 1:2], rowf[:, 0:1], nbefore[:, 0:1], ALU.mult))
                    then(nc.vector.tensor_tensor(row[:], rowf[:, 1:2], m.dst[:, ds(t, 1)], ALU.add))
                    for k in range(K4):
                        nc.vector.tensor_tensor(gsel[:, k, :], same[:], m.e4[:, ds(t, 1), k].to_broadcast([P, P]), ALU.mult)
                    dve.wait_ge(g_w, t + 1)
                    dve.wait_ge(g_rows, 16 * (t + 1))
                    weigh(prod[:, 0, :], psw[0][:, 0, :], rows[:, 0, :])
                    weigh_scalars(prod[:, 0:1, :], psw[0][:, 0:1, :], rows[:, 0:1, :], 1).then_inc(g_prod, 1)

        @block.tensor
        def _(pe):
            miss = pe.value_load(m.misses[0:1, 0:1], min_val=0, max_val=6 * P)

            def hidden(c, i, halves, free):
                pe.wait_ge(es_loaded[c], 32 * i + 16 * halves)
                if free:
                    pe.wait_ge(hid_ready, 2 * i + c)
                r = slice(0, S * halves)
                nc.tensor.matmul(psh[r, 0:CH], m.fc1[r, r], es[r, c, :], start=True, stop=True).then_inc(hid_summed, 1)

            def weights(d, i, tiles, first):
                if not first:
                    pe.wait_ge(prod_ready, DUOS * (i - 1) + d + 1)
                if d < 2:
                    pe.wait_ge(hid_ready, 2 * i + d + 1)
                for j in range(2 * d, min(2 * d + 2, tiles)):
                    r = slice(S * (j // GT), S * (j // GT) + S)
                    col = P * (j % GT)
                    if j == GT:
                        last.then_inc(half_done, 1)
                        pe.wait_ge(half_done, i + 1)
                    last = nc.tensor.matmul(psw[d][:, j % 2, :], hid[r, col:col + P], m.fc2[r, :], start=True, stop=True)
                last.then_inc(w_ready, 1)

            def sums(d, i, tiles, first):
                pe.wait_ge(prod_ready, DUOS * i + d + 1)
                last_tile = min(2 * d + 2, tiles) - 1
                for j in range(2 * d, last_tile + 1):
                    g = j // GT
                    if j % GT == 0 and not first:
                        pe.wait_ge(agg_copied, 2 * i + g - 1)
                    for k in range(K4):
                        for n, piece in enumerate(PICK[k]):
                            at = piece[3]
                            ins = nc.tensor.matmul(psg[g][W * k:W * k + W, at:at + 32 * piece[1]], sel[:, j, k, :],
                                                   picked(prod[:, j, :], piece), start=(j % GT == 0 and n == 0),
                                                   stop=False, skip_group_check=True, tile_position=(0, W * k))
                    if j == last_tile:
                        ins.then_inc(duo_summed, 1)
                    if j % GT == GT - 1:
                        pe.wait_ge(carry_ready[g], i + 1)
                        if g or not first:
                            pe.wait_ge(agg_copied, 2 * i + g)
                        for k in range(K4):
                            ins = nc.tensor.matmul(psg[g][W * k:W * k + W, 0:AW], carry[:, g, k, :],
                                                   m.aggsb[:, 1 - g, :], start=False, stop=True,
                                                   skip_group_check=True, tile_position=(0, W * k))
                        ins.then_inc(group_summed, 1)

            def iteration(i, first, second, following):
                for d in range(DUOS):
                    weights(d, i, 2 * GT, first)
                    if d in (1, 4) and following:
                        hidden(d // 4, i + 1, following, True)
                    if d >= 2:
                        sums(d - 2, i, 2 * GT, first)
                    elif not first:
                        sums(d + 3, i - 1, 2 * GT, second)

            with pe.If(miss == 0):
                for c in range(2):
                    hidden(c, 0, 2, c > 0)
                iteration(0, True, False, 2)
                iteration(1, False, True, 2)
                with pe.Fori(2, PAIRS - 1) as i:
                    iteration(i, False, False, 2)
                iteration(PAIRS - 1, False, False, 1)
                weights(0, PAIRS, GT, False)
                sums(3, PAIRS - 1, 2 * GT, False)
                weights(1, PAIRS, GT, False)
                sums(4, PAIRS - 1, 2 * GT, False)
                weights(2, PAIRS, GT, False)
                for d in range(3):
                    sums(d, PAIRS, GT, False)
            with pe.Else():
                with pe.Fori(0, TILES) as t:
                    pe.wait_ge(g_es, 16 * (t + 1))
                    nc.tensor.matmul(psh[:, 0:P], m.fc1[0:S, :], es[0:S, 0, 0:P], start=True, stop=True).then_inc(g_hid, 1)
                    pe.wait_ge(g_act, t + 1)
                    nc.tensor.matmul(psw[0][:, 0, :], hid[0:S, 0:P], m.fc2[0:S, :], start=True, stop=True).then_inc(g_w, 1)
                    pe.wait_ge(g_prod, t + 1)
                    for k in range(K4):
                        for piece in PICK[k]:
                            at = AW * (k % 2) + piece[3]
                            ins = nc.tensor.matmul(psg[k // 2][:, at:at + 32 * piece[1]], gsel[:, k, :],
                                                   picked(prod[:, 0, :], piece), start=True, stop=True,
                                                   skip_group_check=True)
                    ins.then_inc(g_sum, 1)


def node_block(nc, io, m):
    with ExitStack() as ctx:
        def sb(name, shape, dt=F32):
            return ctx.enter_context(nc.sbuf_tensor(name, shape, dt))

        def sem(name):
            return ctx.enter_context(nc.semaphore(name))

        xs = sb("nxs", [S, 2, CB * P])
        xv = sb("nxv", [3 * V, 2, CB * P])
        xr = sb("nxr", [P, 2, CB, F])
        ag = sb("nag", [P, 2, CB, K4 * AW])
        turned = sb("turned", [P, 2, K4 + 1, P])
        act_s = sb("act_s", [P, 2, S])
        tanh_g = sb("tanh_g", [P, 2, V])
        gate = sb("gate", [P, 2, V])
        stats = sb("stats", [P, 6])
        aggr = sb("aggr", [P, 2])
        y = sb("y", [P, NBLK, F])
        moments = sb("moments", [P, NBLK, 2])
        rstd = sb("rstd", [P, NBLK])
        pst = [ctx.enter_context(nc.psum_tensor(f"pst{s}", [P, 2, 512], F32)) for s in range(2)]
        pso = [ctx.enter_context(nc.psum_tensor(f"pso{s}", [P, 512], F32)) for s in range(2)]

        n_in = [sem(f"n_in{c}") for c in range(2)]
        n_turned = sem("n_turned")
        n_copied_v = sem("n_copied_v")
        n_copied_s = sem("n_copied_s")
        n_lin = sem("n_lin")
        n_act = sem("n_act")
        n_tick = sem("n_tick")
        n_step = sem("n_step")
        n_y = sem("n_y")
        n_clear = sem("n_clear")
        n_var = sem("n_var")
        n_std = sem("n_std")
        n_norm = sem("n_norm")
        n_out = sem("n_out")

        chunks = NBLK // CB
        ITER = 2 * CB
        ITERS = chunks // 2
        block = ctx.enter_context(nc.Block())

        def blocks_of(i):
            return [(i * ITER + q, q // CB, q % CB, P) for q in range(ITER)]

        rest = [(ITERS * ITER, 0, 0, P), (ITERS * ITER + 1, 0, 1, LASTN)]

        @block.sync
        def _(sp):
            def load(c, i):
                at = (2 * i + c) * (CB * P)
                for dst, src in ((ag, m.agg), (xr, io["x"])):
                    sp.dma_start(dst[:, c, :, :], src[ds(at, CB * P), :].rearrange("(b p) f -> p b f", p=P)).then_inc(n_in[c], 16)
                sp.dma_start(xs[:, c, :], io["xT"][0:S, ds(at, CB * P)]).then_inc(n_in[c], 16)
                sp.dma_start(xv[:, c, :], io["xT"][S:F, ds(at, CB * P)]).then_inc(n_in[c], 16)

            for c in range(2):
                load(c, 0)
            with sp.Fori(1, ITERS) as i:
                for c in range(2):
                    sp.wait_ge(n_y, CB * (2 * i + c - 1))
                    sp.sem_inc(n_tick, 1)
                    load(c, i)
            sp.wait_ge(n_y, CB * (2 * ITERS - 1))
            for n, _c, b, width in rest:
                r = slice(n * P, n * P + width)
                sp.dma_start(ag[0:width, 0, b, :], m.agg[r, :]).then_inc(n_in[0], 16)
                sp.dma_start(xr[0:width, 0, b, :], io["x"][r, :]).then_inc(n_in[0], 16)
                sp.dma_start(xs[:, 0, b * P:b * P + width], io["xT"][0:S, r]).then_inc(n_in[0], 16)
                sp.dma_start(xv[:, 0, b * P:b * P + width], io["xT"][S:F, r]).then_inc(n_in[0], 16)
            with sp.Fori(0, chunks) as i:
                sp.wait_ge(n_norm, CB * (i + 1))
                sp.sem_inc(n_tick, 1)
                sp.dma_start(io["out"][ds(i * (CB * P), CB * P), :].rearrange("(b p) f -> p b f", p=P),
                             y[:, ds(i * CB, CB), :]).then_inc(n_out, 16)
            sp.wait_ge(n_norm, NBLK)
            for n, _c, _b, width in rest:
                sp.dma_start(io["out"][n * P:n * P + width, :], y[0:width, n, :]).then_inc(n_out, 16)
            sp.wait_ge(n_out, 16 * (chunks + 2))

        @block.tensor
        def _(pe):
            def turn(blk, free):
                n, c, b, width = blk
                s = b % 2
                if free:
                    pe.wait_ge(n_copied_v, n - 1)
                    pe.wait_ge(n_copied_s, n - 1)
                rows = ag[0:width, c, b, :]
                eye = m.ident[0:width, 0:width]
                for q in range(K4 + 1):
                    at = P * (q % 3)
                    ins = nc.tensor.transpose(pst[s][:, q // 3, at:at + width], rows[:, P * q:P * q + P], eye)
                ins.then_inc(n_turned, 1)

            def lin2(blk, free):
                n, c, b, width = blk
                s = b % 2
                pe.wait_ge(n_copied_v, n + 1)
                pe.wait_ge(n_copied_s, n + 1)
                if free:
                    pe.wait_ge(n_y, n - 1)
                nodes = slice(b * P, b * P + width)
                both, outs, outv = (pso[s][0:width, x:y] for x, y in ((0, 2 * SO), (0, SO), (SO, 2 * SO)))
                steps = [(both, turned[:, s, 0, 0:width], m.m0[:]), (outs, turned[:, s, K4, 0:width], m.m4[:]),
                         (outs, xs[:, c, nodes], m.mscs[:])]
                steps += [(outv, turned[:, s, i + 1, 0:width], m.mv[:, i, :]) for i in range(3)]
                steps += [(outv, xv[:, c, nodes], m.mscv[:])]
                for q, (out, left, right) in enumerate(steps):
                    ins = nc.tensor.matmul(out, left, right, start=(q == 0), stop=(q == len(steps) - 1), skip_group_check=True)
                ins.then_inc(n_lin, 1)

            def iteration(i, first):
                todo = blocks_of(i)
                for q, blk in enumerate(todo):
                    if q == 0:
                        pe.wait_ge(n_in[0], 64 * (i + 1))
                    if q == CB:
                        pe.wait_ge(n_in[1], 64 * (i + 1))
                    turn(blk, not first or q >= 2)
                    if q:
                        lin2(todo[q - 1], not first or q >= 3)
                    elif not first:
                        lin2((i * ITER - 1, 1, CB - 1, P), True)

            iteration(0, True)
            with pe.Fori(1, ITERS) as i:
                iteration(i, False)
            pe.wait_ge(n_in[0], 64 * ITERS + 128)
            turn(rest[0], True)
            lin2((ITERS * ITER - 1, 1, CB - 1, P), True)
            turn(rest[1], True)
            lin2(rest[0], True)
            lin2(rest[1], True)

        @block.scalar
        def _(act):
            def copy(blk, free):
                n, _c, b, width = blk
                s = b % 2
                act.wait_ge(n_turned, n + 1)
                if free:
                    act.wait_ge(n_lin, n - 1)
                src = pst[s][:, 1, 0:2 * P].rearrange("p (i n) -> p i n", i=2)[:, :, 0:width]
                nc.scalar.activation(turned[:, s, 3:5, 0:width], src, ACT.Copy).then_inc(n_copied_s, 1)

            def gates(blk):
                n, _c, b, width = blk
                s = b % 2
                act.wait_ge(n_lin, n + 1)
                act.sem_inc(n_tick, 1)
                col = ds(n, 1)
                nc.scalar.activation(act_s[0:width, s, :], pso[s][0:width, 0:S], ACT.Silu, scale=m.a[0:width, col])
                nc.scalar.activation(tanh_g[0:width, s, :], pso[s][0:width, S:SO], ACT.Tanh,
                                     scale=m.ahalf[0:width, col]).then_inc(n_act, 1)

            def iteration(i, first):
                todo = blocks_of(i)
                for q, blk in enumerate(todo):
                    copy(blk, not first or q >= 2)
                    if q:
                        gates(todo[q - 1])
                    elif not first:
                        gates((i * ITER - 1, 1, CB - 1, P))

            iteration(0, True)
            with act.Fori(1, ITERS) as i:
                iteration(i, False)
            copy(rest[0], True)
            gates((ITERS * ITER - 1, 1, CB - 1, P))
            copy(rest[1], True)
            gates(rest[0])
            gates(rest[1])
            act.wait_ge(n_var, 1)
            nc.scalar.activation(rstd[:], rstd[:], ACT.Sqrt).then_inc(n_std, 1)

        @block.vector
        def _(dve):
            nc.vector.memset(moments[:], 0.0).then_inc(n_clear, 1)
            dve.wait_ge(n_clear, 1)
            STEPS = 5

            def copy(blk, free):
                n, _c, b, width = blk
                s = b % 2
                dve.wait_ge(n_turned, n + 1)
                if free:
                    dve.wait_ge(n_lin, n - 1)
                src = pst[s][:, 0, 0:3 * P].rearrange("p (i n) -> p i n", i=3)[:, :, 0:width]
                nc.vector.tensor_copy(turned[:, s, 0:3, 0:width], src).then_inc(n_copied_v, 1)

            def finish(blk):
                n, c, b, width = blk
                s = b % 2
                r = slice(0, width)
                step = [0]

                def then(ins):
                    ins.then_inc(n_step, 1)
                    step[0] += 1
                    dve.wait_ge(n_step, n * STEPS + step[0])

                row = y[r, ds(n, 1), :].rearrange("p o f -> p (o f)")
                vec = row[:, S:F].rearrange("p (d i) -> p d i", i=3)
                dve.wait_ge(n_act, n + 1)
                then(nc.vector.tensor_scalar(gate[r, s, :], tanh_g[r, s, :], 0.5, 0.5, ALU.mult, ALU.add))
                nc.vector.tensor_tensor(row[:, 0:S], act_s[r, s, :], xr[r, c, b, 0:S], ALU.add)
                then(nc.vector.scalar_tensor_tensor(
                    vec, pso[s][r, SO:2 * SO].rearrange("p (d i) -> p d i", i=3), m.a[r, ds(n, 1)],
                    gate[r, s, :].unsqueeze(2).to_broadcast([width, V, 3]), ALU.mult, ALU.mult))
                then(nc.vector.tensor_tensor(row[:, S:F], row[:, S:F], xr[r, c, b, S:F], ALU.add))
                dve.sem_inc(n_tick, 1)
                then(nc.vector.bn_stats(stats[r, :], row))
                dve.sem_inc(n_tick, 1)
                then(nc.vector.bn_aggr(aggr[r, :], stats[r, :]))
                dve.sem_inc(n_tick, 1)
                nc.vector.tensor_copy(moments[r, ds(n, 1), :], aggr[r, :].unsqueeze(1)).then_inc(n_y, 1)

            def iteration(i, first):
                todo = blocks_of(i)
                for q, blk in enumerate(todo):
                    copy(blk, not first or q >= 2)
                    if q:
                        finish(todo[q - 1])
                    elif not first:
                        finish((i * ITER - 1, 1, CB - 1, P))

            iteration(0, True)
            with dve.Fori(1, ITERS) as i:
                iteration(i, False)
            copy(rest[0], True)
            finish((ITERS * ITER - 1, 1, CB - 1, P))
            copy(rest[1], True)
            finish(rest[0])
            finish(rest[1])
            dve.wait_ge(n_y, NBLK)
            nc.vector.tensor_scalar(rstd[:], moments[:, :, 1], EPS, None, ALU.add).then_inc(n_var, 1)
            dve.wait_ge(n_std, 1)
            nc.vector.reciprocal(rstd[:], rstd[:]).then_inc(n_var, 1)
            dve.wait_ge(n_var, 2)

            def normalize(n, width):
                row = y[0:width, ds(n, 1), :].rearrange("p o f -> p (o f)")
                nc.vector.tensor_scalar(row, row, moments[0:width, ds(n, 1), 0], rstd[0:width, ds(n, 1)],
                                        ALU.subtract, ALU.mult).then_inc(n_norm, 1)

            with dve.Fori(0, chunks) as i:
                for b in range(CB):
                    normalize(i * CB + b, P)
            for n, _c, _b, width in rest:
                normalize(n, width)


def build(nc, io):
    with ExitStack() as ctx:
        def sb(name, shape, dt=F32):
            return ctx.enter_context(nc.sbuf_tensor(name, shape, dt))

        m = Shared()
        m.h = nc.dram_tensor("h_table", (N, F), F32).ap()
        m.agg = nc.dram_tensor("agg_table", (AGG_ROWS, K4 * AW), F32).ap()
        m.src = sb("src_cols", [P, TILES], I32)
        m.dst = sb("dst_cols", [P, TILES], I32)
        m.local = sb("dst_in_window", [P, TILES])
        m.e4 = sb("e4_cols", [P, TILES, K4])
        m.base = sb("window_base", [1, GROUPS], I32)
        m.delta = sb("window_step", [P, GROUPS])
        m.misses = sb("misses", [1, 1], I32)
        m.a = sb("a_cols", [P, NBLK])
        m.ahalf = sb("a_half", [P, NBLK])
        m.ident = sb("ident", [P, P])
        m.earlier = sb("earlier", [P, P])
        m.win = sb("win", [P, W])
        m.shift = sb("shift", [P, K4, W])
        m.spare = sb("spare", [P, 1], I32)
        m.fc1 = sb("fc1", [P, P])
        m.fc2 = sb("fc2", [P, WN])
        m.mscs = sb("mscs", [S, SO])
        m.mscv = sb("mscv", [3 * V, 3 * V])
        m.m0 = sb("m0", [P, 2 * SO])
        m.m4 = sb("m4", [P, SO])
        m.mv = sb("mv", [P, 3, 3 * V])
        m.aggsb = sb("aggsb", [P, 2, AW])
        setup_block(nc, io, m)
        edge_block(nc, io, m)
        node_block(nc, io, m)


def kernel(x, src, dst, edge_attr_4, edge_attr_64, node_vec1, L0_gnn_lin1_ws, L0_gnn_lin1_wv, L0_gnn_fc_w1,
           L0_gnn_fc_w2, L0_gnn_sc_ws, L0_gnn_sc_wv, L0_gnn_lin2_ws, L0_gnn_lin2_wv):
    import concourse.bacc as bacc
    from concourse.bass_utils import run_bass_kernel_spmd

    x, src, dst = np.asarray(x), np.asarray(src), np.asarray(dst)
    e4, es = np.asarray(edge_attr_4), np.asarray(edge_attr_64)
    xT = np.concatenate([x[:, :S].T, x[:, S:].reshape(N, V, 3).transpose(2, 1, 0).reshape(3 * V, N)])
    arrays = {
        "x": x, "xT": xT,
        "srcT": src.reshape(TILES, P).T, "dstT": dst.reshape(TILES, P).T, "dst": dst.reshape(TILES, P),
        "e4T": e4.reshape(TILES, P, K4).transpose(1, 0, 2), "esT": es.T,
        "node_vec": node_vec1, "lin1_ws": L0_gnn_lin1_ws, "lin1_wv": L0_gnn_lin1_wv, "fc_w1": L0_gnn_fc_w1,
        "fc_w2": L0_gnn_fc_w2, "sc_ws": L0_gnn_sc_ws, "sc_wv": L0_gnn_sc_wv, "lin2_ws": L0_gnn_lin2_ws,
        "lin2_wv": L0_gnn_lin2_wv,
    }
    nc = bacc.Bacc("TRN2", target_bir_lowering=False, num_devices=1)
    io, launch = {}, {}
    for name, a in arrays.items():
        a = np.ascontiguousarray(a)
        launch[f"in_{name}"] = a
        io[name] = nc.dram_tensor(f"in_{name}", a.shape, mybir.dt.from_np(a.dtype), kind="ExternalInput").ap()
    io["out"] = nc.dram_tensor("out", (N, F), F32, kind="ExternalOutput").ap()
    build(nc, io)
    return run_bass_kernel_spmd(nc, [launch], core_ids=[0]).results[0]["out"]
```
